# Optimizing a Trainium2 kernel written in Bass

```python
import numpy as np
import jax
import jax.numpy as jnp

def _softmax(x, axis=-1):
    return jax.nn.softmax(x, axis=axis)

def _gelu(x):
    return jax.nn.gelu(x, approximate=True)

def _silu(x):
    return jax.nn.silu(x)

def _sigmoid(x):
    return jax.nn.sigmoid(x)

def _layernorm(x, axis=-1, eps=1e-05):
    m = jnp.mean(x, axis=axis, keepdims=True)
    v = jnp.var(x, axis=axis, keepdims=True)
    return (x - m) / jnp.sqrt(v + eps)

def _scatter_add(tgt, idx, src, axis=0):
    return tgt.at[idx].add(src)

def _segment_sum(src, seg, n):
    return jax.ops.segment_sum(src, seg, n)
kernel_name = 'mk_adj_resnorm_d1_adj_r2_91486c'

def setup_inputs(seed: int=0):
    np.random.seed(seed)
    _w = jnp.asarray

    def _rec_inputs():
        import jax
        import jax.numpy as jnp
        _gk = jax.random.key(seed)
        x = -0.0005207 + 1.001 * jax.random.normal(jax.random.fold_in(_gk, 1), (4096, 128), jnp.float32)
        _w = (1.0 + jnp.arange(4096, dtype=jnp.float32)) ** (-0.5)
        _w = _w / _w.mean()
        _pij = jnp.clip(0.000976562 * _w[:, None] * _w[None, :], 0.0, 1.0)
        _a = jax.random.uniform(jax.random.fold_in(_gk, 2), (4096, 4096)) < _pij
        _a = jnp.logical_or(_a, jnp.eye(4096, dtype=bool))
        _af = _a.astype(jnp.float32)
        _af = _af * jax.random.uniform(jax.random.fold_in(_gk, 3), (4096, 4096), jnp.float32, 0.05, 1)
        adj = _af
        return (x, adj)
    x, adj = _rec_inputs()

    def _L0_gnn_setup():
        import jax, jax.numpy as jnp
        import numpy as np
        N = 4096
        D = 128
        L = 3

        def _cxin_conv(x, a, eps, W, b):
            ax = a @ x
            h = ax + (1.0 + eps[0]) * ax
            for i in range(L):
                h = jax.nn.relu(h @ W[i].T + b[i])
            return h
        key = jax.random.key(seed)
        ks = jax.random.split(key, 8)
        s = 1.0 / np.sqrt(D)
        return {'x1': jax.random.normal(ks[0], (N, D), jnp.float32), 'x2': jax.random.normal(ks[1], (N, D), jnp.float32), 'G1': jax.random.uniform(ks[2], (N, N), jnp.float32), 'G2': jax.random.uniform(ks[3], (N, N), jnp.float32), 'eps1': jnp.zeros((1,), jnp.float32), 'eps2': jnp.zeros((1,), jnp.float32), 'W1': jax.random.normal(ks[4], (L, D, D), jnp.float32) * s, 'b1': jnp.zeros((L, D), jnp.float32), 'W2': jax.random.normal(ks[5], (L, D, D), jnp.float32) * s, 'b2': jnp.zeros((L, D), jnp.float32), 'Wm': jax.random.normal(ks[6], (D, 2 * D), jnp.float32) * (1.0 / np.sqrt(2 * D)), 'bm': jnp.zeros((D,), jnp.float32)}
    _L0_gnn_all = _L0_gnn_setup()
    _L0_gnn_in = {k: v for k, v in _L0_gnn_all.items() if k in ('x2', 'eps1', 'eps2', 'W1', 'b1', 'W2', 'b2', 'Wm', 'bm')}
    del _L0_gnn_all
    return {'x': x, 'adj': adj, 'L0_gnn_x2': _L0_gnn_in['x2'], 'L0_gnn_eps1': _L0_gnn_in['eps1'], 'L0_gnn_eps2': _L0_gnn_in['eps2'], 'L0_gnn_W1': _L0_gnn_in['W1'], 'L0_gnn_b1': _L0_gnn_in['b1'], 'L0_gnn_W2': _L0_gnn_in['W2'], 'L0_gnn_b2': _L0_gnn_in['b2'], 'L0_gnn_Wm': _L0_gnn_in['Wm'], 'L0_gnn_bm': _L0_gnn_in['bm']}

def reference(x, adj, L0_gnn_x2, L0_gnn_eps1, L0_gnn_eps2, L0_gnn_W1, L0_gnn_b1, L0_gnn_W2, L0_gnn_b2, L0_gnn_Wm, L0_gnn_bm):
    import jax
    import jax.numpy as jnp

    def _L0_gnn_ref(x1, x2, G1, G2, eps1, eps2, W1, b1, W2, b2, Wm, bm):
        import jax, jax.numpy as jnp
        import numpy as np
        N = 4096
        D = 128
        L = 3

        def _cxin_conv(x, a, eps, W, b):
            ax = a @ x
            h = ax + (1.0 + eps[0]) * ax
            for i in range(L):
                h = jax.nn.relu(h @ W[i].T + b[i])
            return h
        out1 = _cxin_conv(x1, G1, eps1, W1, b1)
        out2 = _cxin_conv(x2, G2, eps2, W2, b2)
        merged = jnp.concatenate((out1, out2), axis=1)
        return merged @ Wm.T + bm
    x = _layernorm(x + _L0_gnn_ref(x, L0_gnn_x2, adj, adj, L0_gnn_eps1, L0_gnn_eps2, L0_gnn_W1, L0_gnn_b1, L0_gnn_W2, L0_gnn_b2, L0_gnn_Wm, L0_gnn_bm), axis=-1)
    return x

_drawn_inputs = setup_inputs


def setup_inputs(seed=0):
    import zlib

    import numpy as np

    out = dict(_drawn_inputs(seed))
    spreads = {'L0_gnn_b1': (0.0, 0.1), 'L0_gnn_b2': (0.0, 0.1), 'L0_gnn_bm': (0.0, 0.1)}
    factors = {}
    for name, (base, spread) in spreads.items():
        noise = np.random.default_rng([zlib.crc32(name.encode()), seed]).standard_normal(out[name].shape)
        drawn = base * np.exp(spread * noise) if base else spread * noise
        out[name] = jnp.asarray(drawn.astype(out[name].dtype))
    for name, factor in factors.items():
        out[name] = (out[name] * factor).astype(out[name].dtype)
    return out
```

```python
from contextlib import ExitStack

import concourse.bass as bass
from concourse import mybir

ALU = mybir.AluOpType
ACT = mybir.ActivationFunctionType
F32 = mybir.dt.float32
F32R = mybir.dt.float32r

P = 128
BRANCHES = 2
LN_EPS = 1e-5


def gnn_resnorm_kernel(nc: bass.Bass, adj_tiles, x1, x2, eps, w_in_out, bias_cols, bm, out):
    CHUNKS, UNITS, _, KU, C = adj_tiles.shape
    N, D = x1.shape
    LAYERS = bias_cols.shape[2]
    KT = N // P
    GU = 2
    GROUPS = UNITS // GU
    GK = GU * KU
    RING = 8
    AHEAD = RING // GU
    Q = C // P
    NW = BRANCHES * LAYERS + BRANCHES
    XRING = 2
    assert D == P and UNITS % RING == 0 and C * 4 == 2048

    x_pieces = [x.rearrange("(p k) d -> p k d", p=P) for x in (x1, x2)]
    rows = "(c m q) d -> c m (q d)"
    x_rows = x1.rearrange(rows, c=CHUNKS, q=Q)
    out_rows = out.rearrange(rows, c=CHUNKS, q=Q)

    with ExitStack() as ctx:
        def sb(name, shape, dt=F32):
            return ctx.enter_context(nc.sbuf_tensor(name, shape, dt))

        def psum(name):
            return ctx.enter_context(nc.psum_tensor(name, [P, C], F32))

        def sem(name):
            return ctx.enter_context(nc.semaphore(name))

        adj_raw = sb("adj_raw", [P, RING, KU * C])
        adj_hi = sb("adj_hi", [P, RING, KU * C], F32R)
        adj_lo = sb("adj_lo", [P, RING, KU * C], F32R)
        x_raw = sb("x_raw", [P, XRING, BRANCHES, GK, D])
        x_hi = sb("x_hi", [P, BRANCHES, KT, D], F32R)
        x_lo = sb("x_lo", [P, BRANCHES, KT, D], F32R)
        w_raw = sb("w_raw", [P, NW, D])
        w_hi = sb("w_hi", [P, NW, D], F32R)
        w_lo = sb("w_lo", [P, NW, D], F32R)
        bias = sb("bias", [P, BRANCHES, LAYERS])
        eps_raw = sb("eps_raw", [P, BRANCHES])
        scale = sb("scale", [P, BRANCHES])
        ln_eps = sb("ln_eps", [P, 1])
        bm_rows = sb("bm_rows", [P, Q, D])
        h = sb("h", [P, BRANCHES, C])
        h_hi = sb("h_hi", [P, BRANCHES, C], F32R)
        h_lo = sb("h_lo", [P, BRANCHES, C], F32R)
        resid = sb("resid", [P, C])
        y = sb("y", [P, C])
        normed = sb("normed", [P, C])
        stats = sb("stats", [P, Q, 6])
        mean_var = sb("mean_var", [P, Q, 2])
        std = sb("std", [P, Q])
        rstd = sb("rstd", [P, Q])

        agg = [psum(f"agg{b}") for b in range(BRANCHES)]
        layer = [psum(f"layer{b}") for b in range(BRANCHES)]
        merged = psum("merged")

        adj_loaded = [sem(f"adj_loaded{s}") for s in range(RING)]
        adj_hi_ready = sem("adj_hi_ready")
        adj_lo_ready = sem("adj_lo_ready")
        group_done = sem("group_done")
        x_loaded = [sem(f"x_loaded{s}") for s in range(XRING)]
        x_hi_ready = sem("x_hi_ready")
        x_lo_ready = sem("x_lo_ready")
        w_loaded = sem("w_loaded")
        w_hi_ready = sem("w_hi_ready")
        w_lo_ready = sem("w_lo_ready")
        small_loaded = sem("small_loaded")
        scale_ready = sem("scale_ready")
        ln_eps_ready = sem("ln_eps_ready")
        bm_loaded = sem("bm_loaded")
        agg0_done = sem("agg0_done")
        layer_done = [sem(f"layer_done{b}") for b in range(BRANCHES)]
        h_ready = [sem(f"h_ready{b}") for b in range(BRANCHES)]
        h_hi_ready = [sem(f"h_hi_ready{b}") for b in range(BRANCHES)]
        h_lo_ready = [sem(f"h_lo_ready{b}") for b in range(BRANCHES)]
        merge_done = sem("merge_done")
        resid_loaded = sem("resid_loaded")
        resid_ready = sem("resid_ready")
        y_ready = sem("y_ready")
        stats_ready = sem("stats_ready")
        mean_var_ready = sem("mean_var_ready")
        std_ready = sem("std_ready")
        rstd_ready = sem("rstd_ready")
        normed_ready = sem("normed_ready")
        stored = sem("stored")

        SPLITS = LAYERS + 1

        block = ctx.enter_context(nc.Block())

        @block.sync
        def _(sp):
            def load_unit(c, u):
                if not (isinstance(c, int) and c == 0 and u < RING):
                    sp.wait_ge(adj_lo_ready, c * UNITS + (u - RING + 1))
                sp.dma_start(adj_raw[:, u % RING, :],
                             adj_tiles[bass.ds(c, 1), u].rearrange("a p k i -> p (a k i)")
                             ).then_inc(adj_loaded[u % RING], 16)

            def load_x(g):
                if g >= XRING:
                    sp.wait_ge(x_lo_ready, g - XRING + 1)
                for b in range(BRANCHES):
                    sp.dma_start(x_raw[:, g % XRING, b], x_pieces[b][:, g * GK:(g + 1) * GK, :]
                                 ).then_inc(x_loaded[g % XRING], 16)

            for g in range(GROUPS):
                load_x(g)
                for u in range(g * GU, (g + 1) * GU):
                    load_unit(0, u)
            with sp.Fori(1, CHUNKS) as c:
                for u in range(UNITS):
                    load_unit(c, u)

        @block.gpsimd
        def _(pool):
            pool.dma_start(bm_rows[:, :, :], bm.rearrange("(a q d) -> a q d", a=1, q=1).to_broadcast([P, Q, D])
                           ).then_inc(bm_loaded, 16)
            pool.wait_ge(bm_loaded, 16)

            def residual(c):
                pool.dma_start(resid[:, :], x_rows[bass.ds(c, 1)].rearrange("a m n -> (a m) n")
                               ).then_inc(resid_loaded, 16)
                pool.wait_ge(resid_loaded, c * 16 + 16)
                nc.gpsimd.tensor_tensor(resid[:, :], resid[:, :], bm_rows[:, :, :].rearrange("p q d -> p (q d)"),
                                        ALU.add).then_inc(resid_ready, 1)

            def store(c):
                pool.wait_ge(normed_ready, (c + 1) * Q)
                pool.dma_start(out_rows[bass.ds(c, 1)].rearrange("a m n -> (a m) n"), normed[:, :]
                               ).then_inc(stored, 16)

            residual(0)
            with pool.Fori(1, CHUNKS) as c:
                store(c - 1)
                pool.wait_ge(y_ready, c)
                residual(c)
            store(CHUNKS - 1)
            pool.wait_ge(stored, 16 * CHUNKS)

        @block.scalar
        def _(act):
            def split_x(g):
                act.wait_ge(x_loaded[g % XRING], 16 * BRANCHES * (g // XRING + 1))
                nc.scalar.activation(x_hi[:, :, g * GK:(g + 1) * GK, :], x_raw[:, g % XRING], ACT.Copy
                                     ).then_inc(x_hi_ready, 1)

            def split_group(c, g):
                if not (isinstance(c, int) and c == 0 and g < AHEAD):
                    act.wait_ge(group_done, c * GROUPS + (g - AHEAD + 1))
                for u in range(g * GU, (g + 1) * GU):
                    act.wait_ge(adj_loaded[u % RING], c * (16 * UNITS // RING) + 16 * (u // RING + 1))
                    nc.scalar.activation(adj_hi[:, u % RING, :], adj_raw[:, u % RING, :], ACT.Copy
                                         ).then_inc(adj_hi_ready, 1)

            def split_agg(c):
                for b in range(BRANCHES):
                    if b == 0:
                        act.wait_ge(agg0_done, c + 1)
                    else:
                        act.wait_ge(group_done, (c + 1) * GROUPS)
                    if not (isinstance(c, int) and c == 0):
                        act.wait_ge(merge_done, c)
                    nc.scalar.activation(h_hi[:, b, :], agg[b][:, :], ACT.Copy, scale=scale[:, b:b + 1]
                                         ).then_inc(h_hi_ready[b], 1)

            def relu_layer(c, l):
                for b in range(BRANCHES):
                    act.wait_ge(layer_done[b], c * LAYERS + (l + 1))
                    nc.scalar.activation(h[:, b, :], layer[b][:, :], ACT.Relu, bias=bias[:, b, l:l + 1]
                                         ).then_inc(h_ready[b], 1)
                    act.wait_ge(h_ready[b], c * LAYERS + (l + 1))
                    nc.scalar.activation(h_hi[:, b, :], h[:, b, :], ACT.Copy).then_inc(h_hi_ready[b], 1)

            def deviation(c):
                act.wait_ge(mean_var_ready, (c + 1) * Q)
                nc.scalar.activation(std[:, :], mean_var[:, :, 1], ACT.Sqrt, bias=ln_eps[:, :]
                                     ).then_inc(std_ready, 1)

            act.dma_start(w_raw[:, :, :], w_in_out).then_inc(w_loaded, 16)
            act.dma_start(bias[:, :, :], bias_cols).then_inc(small_loaded, 16)
            act.dma_start(eps_raw[:, :], eps.rearrange("(a b) -> a b", a=1).to_broadcast([P, BRANCHES])
                          ).then_inc(small_loaded, 16)
            for g in range(GROUPS):
                split_x(g)
                split_group(0, g)
                if g == 1:
                    act.wait_ge(w_loaded, 16)
                    nc.scalar.activation(w_hi[:, :, :], w_raw[:, :, :], ACT.Copy).then_inc(w_hi_ready, 1)
            act.wait_ge(small_loaded, 32)
            act.wait_ge(scale_ready, 1)
            act.wait_ge(ln_eps_ready, 1)

            with act.Fori(1, CHUNKS) as c:
                for g in range(GROUPS):
                    split_group(c, g)
                    if g == AHEAD - 2:
                        split_agg(c - 1)
                    if AHEAD - 1 <= g < AHEAD - 1 + LAYERS:
                        relu_layer(c - 1, g - (AHEAD - 1))
                deviation(c - 1)
            split_agg(CHUNKS - 1)
            for l in range(LAYERS):
                relu_layer(CHUNKS - 1, l)
            deviation(CHUNKS - 1)

        @block.vector
        def _(dve):
            def split_x(g):
                dve.wait_ge(x_hi_ready, g + 1)
                at = x_hi[:, :, g * GK:(g + 1) * GK, :]
                nc.vector.tensor_tensor(x_lo[:, :, g * GK:(g + 1) * GK, :], x_raw[:, g % XRING], at.bitcast(F32),
                                        ALU.subtract).then_inc(x_lo_ready, 1)

            def split_group(c, g):
                for u in range(g * GU, (g + 1) * GU):
                    dve.wait_ge(adj_hi_ready, c * UNITS + (u + 1))
                    nc.vector.tensor_tensor(adj_lo[:, u % RING, :], adj_raw[:, u % RING, :],
                                            adj_hi[:, u % RING, :].bitcast(F32), ALU.subtract
                                            ).then_inc(adj_lo_ready, 1)

            def split_agg(c):
                for b in range(BRANCHES):
                    dve.wait_ge(h_hi_ready[b], c * SPLITS + 1)
                    nc.vector.scalar_tensor_tensor(h_lo[:, b, :], agg[b][:, :], scale[:, b:b + 1],
                                                   h_hi[:, b, :].bitcast(F32), ALU.mult, ALU.subtract
                                                   ).then_inc(h_lo_ready[b], 1)

            def split_layer(c, l):
                for b in range(BRANCHES):
                    dve.wait_ge(h_hi_ready[b], c * SPLITS + (l + 2))
                    nc.vector.tensor_tensor(h_lo[:, b, :], h[:, b, :], h_hi[:, b, :].bitcast(F32), ALU.subtract
                                            ).then_inc(h_lo_ready[b], 1)

            def add_residual(c):
                dve.wait_ge(merge_done, c + 1)
                dve.wait_ge(resid_ready, c + 1)
                nc.vector.tensor_tensor(y[:, :], merged[:, :], resid[:, :], ALU.add).then_inc(y_ready, 1)
                dve.wait_ge(y_ready, c + 1)
                for q in range(Q):
                    nc.vector.bn_stats(stats[:, q, :], y[:, q * D:(q + 1) * D]).then_inc(stats_ready, 1)

            def aggregate_stats():
                for q in range(Q):
                    nc.vector.bn_aggr(mean_var[:, q, :], stats[:, q, :]).then_inc(mean_var_ready, 1)

            def normalize(c):
                dve.wait_ge(std_ready, c + 1)
                nc.vector.reciprocal(rstd[:, :], std[:, :]).then_inc(rstd_ready, 1)
                dve.wait_ge(rstd_ready, c + 1)
                if not (isinstance(c, int) and c == 0):
                    dve.wait_ge(stored, 16 * c)
                for q in range(Q):
                    nc.vector.tensor_scalar(normed[:, q * D:(q + 1) * D], y[:, q * D:(q + 1) * D],
                                            mean_var[:, q, 0:1], rstd[:, q:q + 1], ALU.subtract, ALU.mult
                                            ).then_inc(normed_ready, 1)

            nc.vector.memset(ln_eps[:, :], LN_EPS).then_inc(ln_eps_ready, 1)
            for g in range(GROUPS):
                split_x(g)
                split_group(0, g)
                if g == 1:
                    dve.wait_ge(w_hi_ready, 1)
                    nc.vector.tensor_tensor(w_lo[:, :, :], w_raw[:, :, :], w_hi[:, :, :].bitcast(F32),
                                            ALU.subtract).then_inc(w_lo_ready, 1)
                    dve.wait_ge(small_loaded, 32)
                    nc.vector.tensor_scalar(scale[:, :], eps_raw[:, :], 1.0, 1.0, ALU.add, ALU.add
                                            ).then_inc(scale_ready, 1)
            dve.wait_ge(scale_ready, 1)

            with dve.Fori(1, CHUNKS) as c:
                for g in range(GROUPS):
                    split_group(c, g)
                    if g == AHEAD - 2:
                        split_agg(c - 1)
                    if AHEAD - 1 <= g < AHEAD - 1 + LAYERS:
                        split_layer(c - 1, g - (AHEAD - 1))
                    if g == AHEAD - 1 + LAYERS:
                        add_residual(c - 1)
                        dve.wait_ge(stats_ready, c * Q)
                aggregate_stats()
                normalize(c - 1)
            split_agg(CHUNKS - 1)
            for l in range(LAYERS):
                split_layer(CHUNKS - 1, l)
            add_residual(CHUNKS - 1)
            dve.wait_ge(stats_ready, CHUNKS * Q)
            aggregate_stats()
            normalize(CHUNKS - 1)

        @block.tensor
        def _(pe):
            def three_passes(acc, hi, lo, at_hi, at_lo, first, last):
                nc.tensor.matmul(acc, hi, at_hi, start=first, stop=False)
                nc.tensor.matmul(acc, hi, at_lo, start=False, stop=False)
                return nc.tensor.matmul(acc, lo, at_hi, start=False, stop=last)

            def multiply(b, units):
                for u in units:
                    for k in range(KU):
                        kt = u * KU + k
                        at = slice(k * C, (k + 1) * C)
                        mm = three_passes(agg[b][:, :], x_hi[:, b, kt, :], x_lo[:, b, kt, :],
                                          adj_hi[:, u % RING, at], adj_lo[:, u % RING, at],
                                          kt == 0, kt == KT - 1)
                return mm

            def group(c, g):
                units = range(g * GU, (g + 1) * GU)
                pe.wait_ge(adj_lo_ready, c * UNITS + (g + 1) * GU)
                for b in range(BRANCHES):
                    if g == 0 and not (isinstance(c, int) and c == 0):
                        pe.wait_ge(h_lo_ready[b], c * SPLITS - (SPLITS - 1))
                    mm = multiply(b, units)
                    if g == GROUPS - 1 and b == 0:
                        mm.then_inc(agg0_done, 1)
                mm.then_inc(group_done, 1)

            def run_layer(c, l):
                for b in range(BRANCHES):
                    pe.wait_ge(h_lo_ready[b], c * SPLITS + (l + 1))
                    w = b * LAYERS + l
                    three_passes(layer[b][:, :], w_hi[:, w, :], w_lo[:, w, :], h_hi[:, b, :], h_lo[:, b, :],
                                 True, True).then_inc(layer_done[b], 1)

            def merge(c):
                if not (isinstance(c, int) and c == 0):
                    pe.wait_ge(y_ready, c)
                for b in range(BRANCHES):
                    pe.wait_ge(h_lo_ready[b], (c + 1) * SPLITS)
                for q in range(Q):
                    at = slice(q * P, (q + 1) * P)
                    for b in range(BRANCHES):
                        w = BRANCHES * LAYERS + b
                        hi, lo = h_hi[:, b, at], h_lo[:, b, at]
                        nc.tensor.matmul(merged[:, at], hi, w_hi[:, w, :], start=b == 0, stop=False)
                        nc.tensor.matmul(merged[:, at], hi, w_lo[:, w, :], start=False, stop=False)
                        mm = nc.tensor.matmul(merged[:, at], lo, w_hi[:, w, :], start=False, stop=b == BRANCHES - 1)
                mm.then_inc(merge_done, 1)

            for g in range(GROUPS):
                pe.wait_ge(x_lo_ready, g + 1)
                group(0, g)
            pe.wait_ge(w_lo_ready, 1)
            with pe.Fori(1, CHUNKS) as c:
                for g in range(GROUPS):
                    group(c, g)
                    if g < LAYERS:
                        run_layer(c - 1, g)
                    if g == LAYERS:
                        merge(c - 1)
            for l in range(LAYERS):
                run_layer(CHUNKS - 1, l)
            merge(CHUNKS - 1)


def kernel(x, adj, L0_gnn_x2, L0_gnn_eps1, L0_gnn_eps2, L0_gnn_W1, L0_gnn_b1, L0_gnn_W2, L0_gnn_b2,
           L0_gnn_Wm, L0_gnn_bm):
    import numpy as np
    import concourse.bacc as bacc
    from concourse.bass_utils import run_bass_kernel_spmd

    N, D = x.shape
    C, KU = 512, 2
    chunks, q, units = N // C, C // P, N // (P * KU)
    adj_tiles = np.asarray(adj).reshape(chunks, P, q, P, units, KU).transpose(0, 4, 3, 5, 2, 1)
    adj_tiles = adj_tiles.reshape(chunks, units, P, KU, C)
    w_layers = np.concatenate([np.asarray(L0_gnn_W1), np.asarray(L0_gnn_W2)]).transpose(2, 0, 1)
    w_merge = np.asarray(L0_gnn_Wm).reshape(D, 2, D).transpose(2, 1, 0)
    arrays = {
        "adj_tiles": adj_tiles,
        "x1": np.asarray(x),
        "x2": np.asarray(L0_gnn_x2),
        "eps": np.concatenate([np.asarray(L0_gnn_eps1), np.asarray(L0_gnn_eps2)]),
        "w_in_out": np.concatenate([w_layers, w_merge], axis=1),
        "bias_cols": np.stack([np.asarray(L0_gnn_b1), np.asarray(L0_gnn_b2)]).transpose(2, 0, 1),
        "bm": np.asarray(L0_gnn_bm),
    }
    arrays = {name: np.ascontiguousarray(a) for name, a in arrays.items()}
    nc = bacc.Bacc("TRN2", target_bir_lowering=False, num_devices=1)
    args = [nc.dram_tensor(name, a.shape, mybir.dt.from_np(a.dtype), kind="ExternalInput").ap()
            for name, a in arrays.items()]
    args.append(nc.dram_tensor("out", (N, D), F32, kind="ExternalOutput").ap())
    gnn_resnorm_kernel(nc, *args)
    return run_bass_kernel_spmd(nc, [arrays], core_ids=[0]).results[0]["out"]
```

```python
from contextlib import ExitStack

import concourse.bass as bass
from concourse import mybir

ALU = mybir.AluOpType
ACT = mybir.ActivationFunctionType
F32 = mybir.dt.float32
F32R = mybir.dt.float32r
BF16 = mybir.dt.bfloat16

P = 128
BRANCHES = 2
LN_EPS = 1e-5


def gnn_resnorm_kernel(nc: bass.Bass, adj_tiles, x1, x2, eps, w_in_out, bias_cols, bm, out):
    CHUNKS, UNITS, _, KU, C = adj_tiles.shape
    N, D = x1.shape
    LAYERS = bias_cols.shape[2]
    KT = N // P
    GU = 2
    GROUPS = UNITS // GU
    RING = 8
    AHEAD = RING // GU
    Q = C // P
    NW = BRANCHES * LAYERS + BRANCHES
    XRING = 4
    SPLITS = LAYERS + 1
    LAST = CHUNKS - 1
    FIRST_RELU = AHEAD - 2
    WARM_UP = 9
    assert D == P and UNITS % RING == 0 and C * 4 == 2048

    WHOLE = slice(0, C)
    LEFT, RIGHT = slice(0, C // 2), slice(C // 2, C)
    BR0, BR1, BR1_RIGHT = range(3)
    branch = [0, 1, 1]

    x_units = [x.rearrange("(p k) d -> p k d", p=P) for x in (x1, x2)]
    rows = "(c m q) d -> c m q d"
    x_rows = x1.rearrange(rows, c=CHUNKS, q=Q)
    out_rows = out.rearrange(rows, c=CHUNKS, q=Q)

    with ExitStack() as ctx:
        def sb(name, shape, dt=F32):
            return ctx.enter_context(nc.sbuf_tensor(name, shape, dt))

        def psum(name, shape):
            return ctx.enter_context(nc.psum_tensor(name, shape, F32))

        def sem(name):
            return ctx.enter_context(nc.semaphore(name))

        def sems(name, n):
            return [sem(f"{name}{i}") for i in range(n)]

        adj_raw = sb("adj_raw", [P, RING, KU * C])
        adj_hi = sb("adj_hi", [P, RING, KU * C], F32R)
        adj_lo = sb("adj_lo", [P, RING, KU * C], F32R)
        x_raw = sb("x_raw", [P, XRING, BRANCHES, KU, D])
        x_hi = sb("x_hi", [P, BRANCHES, KT, D], F32R)
        x_lo = sb("x_lo", [P, BRANCHES, KT, D], F32R)
        w_raw = sb("w_raw", [P, NW, D])
        w_split = sb("w_split", [P, NW, 2, D], F32R)
        bias = sb("bias", [P, BRANCHES, LAYERS])
        eps_raw = sb("eps_raw", [P, BRANCHES])
        scale = sb("scale", [P, BRANCHES])
        ln_eps = sb("ln_eps", [P, 1])
        bm_rows = sb("bm_rows", [P, 1, D])
        h = sb("h", [P, BRANCHES, C])
        h_hi = sb("h_hi", [P, BRANCHES, C], F32R)
        h_lo = sb("h_lo", [P, BRANCHES, C], F32R)
        resid = sb("resid", [P, Q, D])
        y = sb("y", [P, Q, D])
        normed = sb("normed", [P, Q, D])
        stats = sb("stats", [P, Q, 6])
        mean_var = sb("mean_var", [P, Q, 2])
        std = sb("std", [P, Q])
        rstd = sb("rstd", [P, Q])

        warm = sb("warm", [P, C], BF16)

        agg = [psum(f"agg{s}", [P, C]) for s in range(3)]
        layer = [psum(f"layer{s}", [P, C]) for s in range(3)]
        merged = psum("merged", [P, Q, 2, D])

        adj_loaded = sems("adj_loaded", RING)
        adj_first_loaded = sem("adj_first_loaded")
        adj_first_hi = sem("adj_first_hi")
        adj_hi_ready = sem("adj_hi_ready")
        adj_lo_ready = sem("adj_lo_ready")
        group_done = sem("group_done")
        x_loaded = sems("x_loaded", XRING)
        x_hi_ready = sem("x_hi_ready")
        x_lo_ready = sem("x_lo_ready")
        w_loaded = sem("w_loaded")
        w_hi_ready = sem("w_hi_ready")
        w_lo_ready = sem("w_lo_ready")
        small_loaded = sem("small_loaded")
        scale_ready = sem("scale_ready")
        ln_eps_ready = sem("ln_eps_ready")
        warm_ready = sem("warm_ready")
        bm_loaded = sem("bm_loaded")
        agg0_done = sem("agg0_done")
        agg1_last_done = sems("agg1_last_done", 2)
        layer_done = sems("layer_done", 3)
        h_ready = sems("h_ready", 3)
        h_hi_ready = sems("h_hi_ready", 3)
        h_lo_ready = sems("h_lo_ready", 3)
        merge_done = sem("merge_done")
        resid_loaded = sem("resid_loaded")
        resid_ready = sem("resid_ready")
        y_part_ready = sem("y_part_ready")
        y_ready = sem("y_ready")
        stats_ready = sem("stats_ready")
        mean_var_ready = sem("mean_var_ready")
        std_ready = sem("std_ready")
        rstd_ready = sem("rstd_ready")
        normed_ready = sem("normed_ready")
        stored = sem("stored")
        stored_last = sems("stored_last", 2)

        def first(c):
            return isinstance(c, int) and c == 0

        def count(s, c, per_chunk, k):
            return k if s == BR1_RIGHT else c * per_chunk + k

        def halves(c):
            if isinstance(c, int) and c == LAST:
                return [(BR0, WHOLE), (BR1, LEFT), (BR1_RIGHT, RIGHT)]
            return [(BR0, WHOLE), (BR1, WHOLE)]

        def layer_bank(c, s, l):
            return agg[s] if isinstance(c, int) and c == LAST and l % 2 else layer[s]

        block = ctx.enter_context(nc.Block())

        @block.sync
        def _(sp):
            def load_unit(c, u):
                if not (first(c) and u < RING):
                    sp.wait_ge(adj_lo_ready, c * UNITS + (u - RING + 1))
                if first(c) and u == 0:
                    sp.dma_start(adj_raw[:, 0, 0:C], adj_tiles[0, 0, :, 0, :]).then_inc(adj_first_loaded, 16)
                    sp.dma_start(adj_raw[:, 0, C:], adj_tiles[0, 0, :, 1:, :].rearrange("p k i -> p (k i)")
                                 ).then_inc(adj_loaded[0], 16)
                    return
                sp.dma_start(adj_raw[:, u % RING, :],
                             adj_tiles[bass.ds(c, 1), u].rearrange("a p k i -> p (a k i)")
                             ).then_inc(adj_loaded[u % RING], 16)

            def load_x(u):
                if u >= XRING:
                    sp.wait_ge(x_lo_ready, u - XRING + 1)
                for b in range(BRANCHES):
                    sp.dma_start(x_raw[:, u % XRING, b], x_units[b][:, u * KU:(u + 1) * KU, :]
                                 ).then_inc(x_loaded[u % XRING], 16)

            for u in range(UNITS):
                load_x(u)
                load_unit(0, u)
                if u == UNITS - XRING:
                    sp.dma_start(w_raw[:, :, :], w_in_out).then_inc(w_loaded, 16)
                    sp.dma_start(bias[:, :, :], bias_cols).then_inc(small_loaded, 16)
                    sp.dma_start(eps_raw[:, :], eps.rearrange("(a b) -> a b", a=1).to_broadcast([P, BRANCHES])
                                 ).then_inc(small_loaded, 16)
                    sp.dma_start(bm_rows[:, :, :],
                                 bm.rearrange("(a q d) -> a q d", a=1, q=1).to_broadcast([P, 1, D])
                                 ).then_inc(bm_loaded, 16)
            with sp.Fori(1, CHUNKS) as c:
                for u in range(UNITS):
                    load_unit(c, u)
            for half in range(2):
                at = slice(half * Q // 2, (half + 1) * Q // 2)
                sp.wait_ge(normed_ready, LAST * Q + at.stop)
                sp.dma_start(out_rows[LAST][:, at, :], normed[:, at, :]).then_inc(stored_last[half], 16)
            for half in range(2):
                sp.wait_ge(stored_last[half], 16)

        @block.gpsimd
        def _(pool):
            def residual(c):
                pool.dma_start(resid[:, :, :], x_rows[bass.ds(c, 1)].rearrange("a m q d -> (a m) q d")
                               ).then_inc(resid_loaded, 16)
                pool.wait_ge(resid_loaded, c * 16 + 16)
                nc.gpsimd.tensor_tensor(resid[:, :, :], resid[:, :, :], bm_rows[:, :, :].to_broadcast([P, Q, D]),
                                        ALU.add).then_inc(resid_ready, 1)

            def store(c):
                pool.wait_ge(normed_ready, (c + 1) * Q)
                pool.dma_start(out_rows[bass.ds(c, 1)].rearrange("a m q d -> (a m) q d"), normed[:, :, :]
                               ).then_inc(stored, 16)

            pool.wait_ge(bm_loaded, 16)
            residual(0)
            with pool.Fori(1, CHUNKS) as c:
                pool.wait_ge(y_part_ready, c)
                residual(c)
                store(c - 1)
            pool.wait_ge(stored, 16 * LAST)

        @block.scalar
        def _(act):
            def split_x(u):
                act.wait_ge(x_loaded[u % XRING], 16 * BRANCHES * (u // XRING + 1))
                nc.scalar.activation(x_hi[:, :, u * KU:(u + 1) * KU, :], x_raw[:, u % XRING], ACT.Copy
                                     ).then_inc(x_hi_ready, 1)

            def split_unit(c, u):
                start = 0
                if first(c) and u == 0:
                    act.wait_ge(adj_first_loaded, 16)
                    nc.scalar.activation(adj_hi[:, 0, 0:C], adj_raw[:, 0, 0:C], ACT.Copy).then_inc(adj_first_hi, 1)
                    start = C
                act.wait_ge(adj_loaded[u % RING], c * (16 * UNITS // RING) + 16 * (u // RING + 1))
                nc.scalar.activation(adj_hi[:, u % RING, start:], adj_raw[:, u % RING, start:], ACT.Copy
                                     ).then_inc(adj_hi_ready, 1)

            def split_group(c, g):
                if not (first(c) and g < AHEAD):
                    act.wait_ge(group_done, c * GROUPS + (g - AHEAD + 1))
                for u in range(g * GU, (g + 1) * GU):
                    if first(c):
                        split_x(u)
                    split_unit(c, u)

            def split_agg(c, s, at):
                if s == BR0:
                    act.wait_ge(agg0_done, c + 1)
                elif isinstance(c, int) and c == LAST:
                    act.wait_ge(agg1_last_done[s - BR1], 1)
                else:
                    act.wait_ge(group_done, (c + 1) * GROUPS)
                if not first(c):
                    act.wait_ge(merge_done, c)
                b = branch[s]
                nc.scalar.activation(h_hi[:, b, at], agg[s][:, at], ACT.Copy, scale=scale[:, b:b + 1]
                                     ).then_inc(h_hi_ready[s], 1)

            def relu(c, s, at, l):
                b, bank = branch[s], layer_bank(c, s, l)
                act.wait_ge(layer_done[s], count(s, c, LAYERS, l + 1))
                nc.scalar.activation(h_hi[:, b, at], bank[:, at], ACT.Relu, bias=bias[:, b, l:l + 1]
                                     ).then_inc(h_hi_ready[s], 1)
                nc.scalar.activation(h[:, b, at], bank[:, at], ACT.Relu, bias=bias[:, b, l:l + 1]
                                     ).then_inc(h_ready[s], 1)

            def deviation(tiles, stats_count):
                act.wait_ge(mean_var_ready, stats_count)
                nc.scalar.activation(std[:, tiles], mean_var[:, tiles, 1], ACT.Sqrt, bias=ln_eps[:, :]
                                     ).then_inc(std_ready, 1)

            def chunk(c):
                for g in range(GROUPS):
                    split_group(c, g)
                    if g == 0:
                        for s, at in halves(None):
                            split_agg(c - 1, s, at)
                    if FIRST_RELU <= g < FIRST_RELU + LAYERS:
                        for s, at in halves(None):
                            relu(c - 1, s, at, g - FIRST_RELU)
                deviation(slice(0, Q), c * Q)

            act.wait_ge(ln_eps_ready, 1)
            nc.scalar.activation(std[:, 0:1], ln_eps[:, :], ACT.Sqrt)
            for g in range(GROUPS):
                split_group(0, g)
                if g == GROUPS - 1:
                    act.wait_ge(w_loaded, 16)
                    nc.scalar.activation(w_split[:, :, 0, :], w_raw[:, :, :], ACT.Copy).then_inc(w_hi_ready, 1)
            act.wait_ge(small_loaded, 32)
            act.wait_ge(scale_ready, 1)
            with act.Fori(1, LAST) as c:
                chunk(c)
            chunk(LAST)

            br0, left, right = halves(LAST)
            split_agg(LAST, *br0)
            relu(LAST, *br0, 0)
            split_agg(LAST, *left)
            relu(LAST, *br0, 1)
            relu(LAST, *left, 0)
            relu(LAST, *br0, 2)
            relu(LAST, *left, 1)
            split_agg(LAST, *right)
            relu(LAST, *left, 2)
            relu(LAST, *right, 0)
            relu(LAST, *right, 1)
            relu(LAST, *right, 2)
            deviation(slice(0, Q // 2), LAST * Q + Q // 2)
            deviation(slice(Q // 2, Q), CHUNKS * Q)

        @block.vector
        def _(dve):
            def split_x(u):
                dve.wait_ge(x_hi_ready, u + 1)
                at = slice(u * KU, (u + 1) * KU)
                nc.vector.tensor_tensor(x_lo[:, :, at, :], x_raw[:, u % XRING], x_hi[:, :, at, :].bitcast(F32),
                                        ALU.subtract).then_inc(x_lo_ready, 1)

            def split_group(c, g):
                for u in range(g * GU, (g + 1) * GU):
                    if first(c):
                        split_x(u)
                    dve.wait_ge(adj_hi_ready, c * UNITS + (u + 1))
                    nc.vector.tensor_tensor(adj_lo[:, u % RING, :], adj_raw[:, u % RING, :],
                                            adj_hi[:, u % RING, :].bitcast(F32), ALU.subtract
                                            ).then_inc(adj_lo_ready, 1)

            def split_agg(c, s, at):
                b = branch[s]
                dve.wait_ge(h_hi_ready[s], count(s, c, SPLITS, 1))
                nc.vector.scalar_tensor_tensor(h_lo[:, b, at], agg[s][:, at], scale[:, b:b + 1],
                                               h_hi[:, b, at].bitcast(F32), ALU.mult, ALU.subtract
                                               ).then_inc(h_lo_ready[s], 1)

            def split_layer(c, s, at, l):
                b = branch[s]
                dve.wait_ge(h_ready[s], count(s, c, LAYERS, l + 1))
                nc.vector.tensor_tensor(h_lo[:, b, at], h[:, b, at], h_hi[:, b, at].bitcast(F32), ALU.subtract
                                        ).then_inc(h_lo_ready[s], 1)

            def add_residual(c, tiles, n):
                dve.wait_ge(merge_done, n + 1)
                dve.wait_ge(resid_ready, c + 1)
                nc.vector.tensor_tensor(y[:, tiles, :], merged[:, tiles, 0, :], resid[:, tiles, :], ALU.add
                                        ).then_inc(y_part_ready, 1)
                dve.wait_ge(y_part_ready, n + 1)
                nc.vector.tensor_tensor(y[:, tiles, :], merged[:, tiles, 1, :], y[:, tiles, :], ALU.add
                                        ).then_inc(y_ready, 1)

            def row_stats(tiles, n):
                dve.wait_ge(y_ready, n + 1)
                for q in range(tiles.start, tiles.stop):
                    nc.vector.bn_stats(stats[:, q, :], y[:, q, :]).then_inc(stats_ready, 1)

            def aggregate_stats(tiles):
                for q in range(tiles.start, tiles.stop):
                    nc.vector.bn_aggr(mean_var[:, q, :], stats[:, q, :]).then_inc(mean_var_ready, 1)

            def normalize(c, tiles, n):
                dve.wait_ge(std_ready, n + 1)
                nc.vector.reciprocal(rstd[:, tiles], std[:, tiles]).then_inc(rstd_ready, 1)
                dve.wait_ge(rstd_ready, n + 1)
                if not first(c):
                    dve.wait_ge(stored, 16 * c)
                for q in range(tiles.start, tiles.stop):
                    nc.vector.tensor_scalar(normed[:, q, :], y[:, q, :], mean_var[:, q, 0:1], rstd[:, q:q + 1],
                                            ALU.subtract, ALU.mult).then_inc(normed_ready, 1)

            def chunk(c):
                tiles = slice(0, Q)
                for g in range(GROUPS):
                    split_group(c, g)
                    if g == 0:
                        for s, at in halves(None):
                            split_agg(c - 1, s, at)
                    if FIRST_RELU <= g < FIRST_RELU + LAYERS:
                        for s, at in halves(None):
                            split_layer(c - 1, s, at, g - FIRST_RELU)
                    if g == GROUPS - 2:
                        add_residual(c - 1, tiles, c - 1)
                        row_stats(tiles, c - 1)
                        dve.wait_ge(stats_ready, c * Q)
                aggregate_stats(tiles)
                normalize(c - 1, tiles, c - 1)

            nc.vector.memset(warm[:, :].bitcast(F32), 0.0).then_inc(warm_ready, 1)
            nc.vector.memset(ln_eps[:, :], LN_EPS).then_inc(ln_eps_ready, 1)
            for g in range(GROUPS):
                split_group(0, g)
                if g == GROUPS - 1:
                    dve.wait_ge(w_hi_ready, 1)
                    nc.vector.tensor_tensor(w_split[:, :, 1, :], w_raw[:, :, :], w_split[:, :, 0, :].bitcast(F32),
                                            ALU.subtract).then_inc(w_lo_ready, 1)
                    dve.wait_ge(small_loaded, 32)
                    nc.vector.tensor_scalar(scale[:, :], eps_raw[:, :], 1.0, 1.0, ALU.add, ALU.add
                                            ).then_inc(scale_ready, 1)
            dve.wait_ge(scale_ready, 1)
            with dve.Fori(1, LAST) as c:
                chunk(c)
            chunk(LAST)

            br0, left, right = halves(LAST)
            low, high = slice(0, Q // 2), slice(Q // 2, Q)
            split_agg(LAST, *br0)
            split_layer(LAST, *br0, 0)
            split_agg(LAST, *left)
            split_layer(LAST, *br0, 1)
            split_layer(LAST, *left, 0)
            split_layer(LAST, *br0, 2)
            split_layer(LAST, *left, 1)
            split_agg(LAST, *right)
            split_layer(LAST, *left, 2)
            split_layer(LAST, *right, 0)
            split_layer(LAST, *right, 1)
            add_residual(LAST, low, LAST)
            split_layer(LAST, *right, 2)
            row_stats(low, LAST)
            dve.wait_ge(stats_ready, LAST * Q + low.stop)
            aggregate_stats(low)
            add_residual(LAST, high, CHUNKS)
            row_stats(high, CHUNKS)
            dve.wait_ge(stats_ready, CHUNKS * Q)
            aggregate_stats(high)
            normalize(LAST, low, LAST)
            normalize(LAST, high, CHUNKS)

        @block.tensor
        def _(pe):
            def operands(b, u, k, at):
                kt = u * KU + k
                cols = slice(k * C + at.start, k * C + at.stop)
                return (kt, x_hi[:, b, kt, :], x_lo[:, b, kt, :],
                        adj_hi[:, u % RING, cols], adj_lo[:, u % RING, cols])

            def multiply(s, at, units):
                for u in units:
                    for k in range(KU):
                        kt, xh, xl, ah, al = operands(branch[s], u, k, at)
                        nc.tensor.matmul(agg[s][:, at], xh, ah, start=kt == 0, stop=False)
                        nc.tensor.matmul(agg[s][:, at], xh, al, start=False, stop=False)
                        mm = nc.tensor.matmul(agg[s][:, at], xl, ah, start=False, stop=kt == KT - 1)
                return mm

            def unit_by_parts(u):
                pe.wait_ge(x_hi_ready, u + 1)
                for k in range(KU):
                    pe.wait_ge(*((adj_first_hi, 1) if u == 0 and k == 0 else (adj_hi_ready, u + 1)))
                    for b in range(BRANCHES):
                        kt, xh, xl, ah, al = operands(b, u, k, WHOLE)
                        nc.tensor.matmul(agg[b][:, :], xh, ah, start=kt == 0, stop=False)
                pe.wait_ge(x_lo_ready, u + 1)
                for b in range(BRANCHES):
                    for k in range(KU):
                        kt, xh, xl, ah, al = operands(b, u, k, WHOLE)
                        nc.tensor.matmul(agg[b][:, :], xl, ah, start=False, stop=False)
                pe.wait_ge(adj_lo_ready, u + 1)
                for b in range(BRANCHES):
                    for k in range(KU):
                        kt, xh, xl, ah, al = operands(b, u, k, WHOLE)
                        mm = nc.tensor.matmul(agg[b][:, :], xh, al, start=False, stop=False)
                return mm

            def group(c, g):
                pe.wait_ge(adj_lo_ready, c * UNITS + (g + 1) * GU)
                for s, at in halves(c):
                    if g == 0 and not first(c) and s != BR1_RIGHT:
                        pe.wait_ge(h_lo_ready[s], c * SPLITS - (SPLITS - 1))
                    mm = multiply(s, at, range(g * GU, (g + 1) * GU))
                    if g == GROUPS - 1 and s == BR0:
                        mm.then_inc(agg0_done, 1)
                mm.then_inc(group_done, 1)

            def run_layer(c, s, at, l):
                w = branch[s] * LAYERS + l
                w_hi, w_lo = w_split[:, w, 0, :], w_split[:, w, 1, :]
                b, bank = branch[s], layer_bank(c, s, l)
                if l == 0 or bank is not layer_bank(c, s, l - 1):
                    pe.wait_ge(h_hi_ready[s], count(s, c, SPLITS, l + 1))
                else:
                    pe.wait_ge(h_ready[s], count(s, c, LAYERS, l))
                nc.tensor.matmul(bank[:, at], w_lo, h_hi[:, b, at], start=True, stop=False)
                nc.tensor.matmul(bank[:, at], w_hi, h_hi[:, b, at], start=False, stop=False)
                pe.wait_ge(h_lo_ready[s], count(s, c, SPLITS, l + 1))
                nc.tensor.matmul(bank[:, at], w_hi, h_lo[:, b, at], start=False, stop=True
                                 ).then_inc(layer_done[s], 1)

            def merge(c, tiles, streams, done=True):
                for q in range(tiles.start, tiles.stop):
                    cols = slice(q * P, (q + 1) * P)
                    for s in streams:
                        b = branch[s]
                        w = BRANCHES * LAYERS + b
                        if q == tiles.start:
                            pe.wait_ge(h_lo_ready[s], count(s, c, SPLITS, SPLITS))
                        nc.tensor.matmul(merged[:, q, :, :], h_hi[:, b, cols], w_split[:, w, :, :],
                                         start=b == 0, stop=False)
                        mm = nc.tensor.matmul(merged[:, q, 0, :], h_lo[:, b, cols], w_split[:, w, 0, :],
                                              start=False, stop=b == BRANCHES - 1)
                if done:
                    mm.then_inc(merge_done, 1)

            def chunk(c, groups):
                for g in groups:
                    group(c, g)
                    if g < LAYERS:
                        for s, at in halves(None):
                            run_layer(c - 1, s, at, g)
                    if g == LAYERS:
                        if not (isinstance(c, int) and c == 1):
                            pe.wait_ge(y_ready, c - 1)
                        merge(c - 1, slice(0, Q), (BR0, BR1))

            pe.wait_ge(warm_ready, 1)
            for _ in range(WARM_UP):
                nc.tensor.matmul(agg[BR1_RIGHT][:, :], warm[:, 0:P], warm[:, :], start=True, stop=True)
            for u in range(0, UNITS - GU):
                mm = unit_by_parts(u)
                if u % GU == GU - 1:
                    mm.then_inc(group_done, 1)
            pe.wait_ge(x_lo_ready, UNITS)
            group(0, GROUPS - 1)
            pe.wait_ge(w_lo_ready, 1)
            chunk(1, range(GROUPS))
            with nc.Fori(2, LAST, engines=[mybir.EngineType.PE], hint_back_edge=True) as c:
                chunk(c, range(GROUPS))
            chunk(LAST, range(GROUPS - AHEAD))

            br0, left, right = halves(LAST)
            tail = range((GROUPS - AHEAD) * GU, UNITS)
            for u in tail:
                pe.wait_ge(adj_lo_ready, LAST * UNITS + u + 1)
                mm = multiply(*br0, [u])
            mm.then_inc(agg0_done, 1)
            multiply(*left, tail[:4])
            run_layer(LAST, *br0, 0)
            multiply(*left, tail[4:]).then_inc(agg1_last_done[0], 1)
            run_layer(LAST, *br0, 1)
            multiply(*right, tail[:2])
            run_layer(LAST, *left, 0)
            multiply(*right, tail[2:4])
            run_layer(LAST, *br0, 2)
            multiply(*right, tail[4:6])
            run_layer(LAST, *left, 1)
            multiply(*right, tail[6:]).then_inc(agg1_last_done[1], 1)
            run_layer(LAST, *left, 2)
            run_layer(LAST, *right, 0)
            pe.wait_ge(y_ready, LAST)
            merge(LAST, slice(0, 1), (BR0, BR1), done=False)
            run_layer(LAST, *right, 1)
            merge(LAST, slice(1, Q // 2), (BR0, BR1))
            run_layer(LAST, *right, 2)
            merge(LAST, slice(Q // 2, Q), (BR0, BR1_RIGHT))


def kernel(x, adj, L0_gnn_x2, L0_gnn_eps1, L0_gnn_eps2, L0_gnn_W1, L0_gnn_b1, L0_gnn_W2, L0_gnn_b2,
           L0_gnn_Wm, L0_gnn_bm):
    import numpy as np
    import concourse.bacc as bacc
    from concourse.bass_utils import run_bass_kernel_spmd

    N, D = x.shape
    C, KU = 512, 2
    chunks, q, units = N // C, C // P, N // (P * KU)
    adj_tiles = np.asarray(adj).reshape(chunks, P, q, P, units, KU).transpose(0, 4, 3, 5, 2, 1)
    adj_tiles = adj_tiles.reshape(chunks, units, P, KU, C)
    w_layers = np.concatenate([np.asarray(L0_gnn_W1), np.asarray(L0_gnn_W2)]).transpose(2, 0, 1)
    w_merge = np.asarray(L0_gnn_Wm).reshape(D, 2, D).transpose(2, 1, 0)
    arrays = {
        "adj_tiles": adj_tiles,
        "x1": np.asarray(x),
        "x2": np.asarray(L0_gnn_x2),
        "eps": np.concatenate([np.asarray(L0_gnn_eps1), np.asarray(L0_gnn_eps2)]),
        "w_in_out": np.concatenate([w_layers, w_merge], axis=1),
        "bias_cols": np.stack([np.asarray(L0_gnn_b1), np.asarray(L0_gnn_b2)]).transpose(2, 0, 1),
        "bm": np.asarray(L0_gnn_bm),
    }
    arrays = {name: np.ascontiguousarray(a) for name, a in arrays.items()}
    nc = bacc.Bacc("TRN2", target_bir_lowering=False, num_devices=1)
    args = [nc.dram_tensor(name, a.shape, mybir.dt.from_np(a.dtype), kind="ExternalInput").ap()
            for name, a in arrays.items()]
    args.append(nc.dram_tensor("out", (N, D), F32, kind="ExternalOutput").ap())
    gnn_resnorm_kernel(nc, *args)
    return run_bass_kernel_spmd(nc, [arrays], core_ids=[0]).results[0]["out"]
```
